# Optimizing a Trainium2 kernel written in Bass

```python
import numpy as np
import jax
import jax.numpy as jnp

def _softmax(x, axis=-1):
    return jax.nn.softmax(x, axis=axis)

def _gelu(x):
    return jax.nn.gelu(x, approximate=True)

def _silu(x):
    return jax.nn.silu(x)

def _sigmoid(x):
    return jax.nn.sigmoid(x)

def _layernorm(x, axis=-1, eps=1e-05):
    m = jnp.mean(x, axis=axis, keepdims=True)
    v = jnp.var(x, axis=axis, keepdims=True)
    return (x - m) / jnp.sqrt(v + eps)

def _scatter_add(tgt, idx, src, axis=0):
    return tgt.at[idx].add(src)

def _segment_sum(src, seg, n):
    return jax.ops.segment_sum(src, seg, n)
kernel_name = 'mk_dlrm_tower_d1_rec_r8_24e716'

def setup_inputs(seed: int=0):
    np.random.seed(seed)
    _w = jnp.asarray

    def _rec_inputs():
        import jax
        import jax.numpy as jnp
        _tk = jax.random.key(seed)
        ids = jnp.stack([jax.random.randint(jax.random.fold_in(_tk, 200 + f), (512,), 0, v, jnp.int32) for f, v in enumerate([12500, 1250, 1250, 1000, 12500, 125000, 1250, 12500, 1250, 1000, 1000, 1250, 12500, 12500, 1250, 1000, 1000, 1000, 1250, 12500, 1250, 1000, 12500, 12500, 1000, 1000])], axis=1)
        tbl_0 = 0.05 * jax.random.normal(jax.random.fold_in(_tk, 500 + 0), (12500, 128), jnp.float32)
        tbl_1 = 0.05 * jax.random.normal(jax.random.fold_in(_tk, 500 + 1), (1250, 128), jnp.float32)
        tbl_2 = 0.05 * jax.random.normal(jax.random.fold_in(_tk, 500 + 2), (1250, 128), jnp.float32)
        tbl_3 = 0.05 * jax.random.normal(jax.random.fold_in(_tk, 500 + 3), (1000, 128), jnp.float32)
        tbl_4 = 0.05 * jax.random.normal(jax.random.fold_in(_tk, 500 + 4), (12500, 128), jnp.float32)
        tbl_5 = 0.05 * jax.random.normal(jax.random.fold_in(_tk, 500 + 5), (125000, 128), jnp.float32)
        tbl_6 = 0.05 * jax.random.normal(jax.random.fold_in(_tk, 500 + 6), (1250, 128), jnp.float32)
        tbl_7 = 0.05 * jax.random.normal(jax.random.fold_in(_tk, 500 + 7), (12500, 128), jnp.float32)
        tbl_8 = 0.05 * jax.random.normal(jax.random.fold_in(_tk, 500 + 8), (1250, 128), jnp.float32)
        tbl_9 = 0.05 * jax.random.normal(jax.random.fold_in(_tk, 500 + 9), (1000, 128), jnp.float32)
        tbl_10 = 0.05 * jax.random.normal(jax.random.fold_in(_tk, 500 + 10), (1000, 128), jnp.float32)
        tbl_11 = 0.05 * jax.random.normal(jax.random.fold_in(_tk, 500 + 11), (1250, 128), jnp.float32)
        tbl_12 = 0.05 * jax.random.normal(jax.random.fold_in(_tk, 500 + 12), (12500, 128), jnp.float32)
        tbl_13 = 0.05 * jax.random.normal(jax.random.fold_in(_tk, 500 + 13), (12500, 128), jnp.float32)
        tbl_14 = 0.05 * jax.random.normal(jax.random.fold_in(_tk, 500 + 14), (1250, 128), jnp.float32)
        tbl_15 = 0.05 * jax.random.normal(jax.random.fold_in(_tk, 500 + 15), (1000, 128), jnp.float32)
        tbl_16 = 0.05 * jax.random.normal(jax.random.fold_in(_tk, 500 + 16), (1000, 128), jnp.float32)
        tbl_17 = 0.05 * jax.random.normal(jax.random.fold_in(_tk, 500 + 17), (1000, 128), jnp.float32)
        tbl_18 = 0.05 * jax.random.normal(jax.random.fold_in(_tk, 500 + 18), (1250, 128), jnp.float32)
        tbl_19 = 0.05 * jax.random.normal(jax.random.fold_in(_tk, 500 + 19), (12500, 128), jnp.float32)
        tbl_20 = 0.05 * jax.random.normal(jax.random.fold_in(_tk, 500 + 20), (1250, 128), jnp.float32)
        tbl_21 = 0.05 * jax.random.normal(jax.random.fold_in(_tk, 500 + 21), (1000, 128), jnp.float32)
        tbl_22 = 0.05 * jax.random.normal(jax.random.fold_in(_tk, 500 + 22), (12500, 128), jnp.float32)
        tbl_23 = 0.05 * jax.random.normal(jax.random.fold_in(_tk, 500 + 23), (12500, 128), jnp.float32)
        tbl_24 = 0.05 * jax.random.normal(jax.random.fold_in(_tk, 500 + 24), (1000, 128), jnp.float32)
        tbl_25 = 0.05 * jax.random.normal(jax.random.fold_in(_tk, 500 + 25), (1000, 128), jnp.float32)
        _rk = jax.random.fold_in(_tk, 7)
        r_dense_features = -0.000520686 + 1.00062 * jax.random.normal(jax.random.fold_in(_rk, 101), (512, 128), jnp.float32)
        W_top1 = 0.0405887 * jax.random.normal(jax.random.fold_in(_tk, 801), (607, 512), jnp.float32)
        W_top2 = 0.0441942 * jax.random.normal(jax.random.fold_in(_tk, 802), (512, 256), jnp.float32)
        W_top3 = 0.0625 * jax.random.normal(jax.random.fold_in(_tk, 803), (256, 1), jnp.float32)
        b_top1 = jnp.zeros((512,), jnp.float32)
        b_top2 = jnp.zeros((256,), jnp.float32)
        return (r_dense_features, ids, tbl_0, tbl_1, tbl_2, tbl_3, tbl_4, tbl_5, tbl_6, tbl_7, tbl_8, tbl_9, tbl_10, tbl_11, tbl_12, tbl_13, tbl_14, tbl_15, tbl_16, tbl_17, tbl_18, tbl_19, tbl_20, tbl_21, tbl_22, tbl_23, tbl_24, tbl_25, W_top1, b_top1, W_top2, b_top2, W_top3)
    r_dense_features, ids, tbl_0, tbl_1, tbl_2, tbl_3, tbl_4, tbl_5, tbl_6, tbl_7, tbl_8, tbl_9, tbl_10, tbl_11, tbl_12, tbl_13, tbl_14, tbl_15, tbl_16, tbl_17, tbl_18, tbl_19, tbl_20, tbl_21, tbl_22, tbl_23, tbl_24, tbl_25, W_top1, b_top1, W_top2, b_top2, W_top3 = _rec_inputs()

    def _L0_rec_setup():
        import jax, jax.numpy as jnp
        import numpy as np
        NUM_SPARSE = 26
        EMBED_DIM = 128
        BATCH = 2048
        key = jax.random.key(seed)
        k1, k2 = jax.random.split(key)
        dense_features = jax.random.normal(k1, (BATCH, EMBED_DIM), dtype=jnp.float32)
        sparse_features = jax.random.normal(k2, (BATCH, NUM_SPARSE, EMBED_DIM), dtype=jnp.float32)
        return {'dense_features': dense_features, 'sparse_features': sparse_features}
    _L0_rec_all = _L0_rec_setup()
    _L0_rec_in = {k: v for k, v in _L0_rec_all.items() if k in ()}
    del _L0_rec_all
    return {'r_dense_features': r_dense_features, 'ids': ids, 'tbl_0': tbl_0, 'tbl_1': tbl_1, 'tbl_2': tbl_2, 'tbl_3': tbl_3, 'tbl_4': tbl_4, 'tbl_5': tbl_5, 'tbl_6': tbl_6, 'tbl_7': tbl_7, 'tbl_8': tbl_8, 'tbl_9': tbl_9, 'tbl_10': tbl_10, 'tbl_11': tbl_11, 'tbl_12': tbl_12, 'tbl_13': tbl_13, 'tbl_14': tbl_14, 'tbl_15': tbl_15, 'tbl_16': tbl_16, 'tbl_17': tbl_17, 'tbl_18': tbl_18, 'tbl_19': tbl_19, 'tbl_20': tbl_20, 'tbl_21': tbl_21, 'tbl_22': tbl_22, 'tbl_23': tbl_23, 'tbl_24': tbl_24, 'tbl_25': tbl_25, 'W_top1': W_top1, 'b_top1': b_top1, 'W_top2': W_top2, 'b_top2': b_top2, 'W_top3': W_top3}

def reference(r_dense_features, ids, tbl_0, tbl_1, tbl_2, tbl_3, tbl_4, tbl_5, tbl_6, tbl_7, tbl_8, tbl_9, tbl_10, tbl_11, tbl_12, tbl_13, tbl_14, tbl_15, tbl_16, tbl_17, tbl_18, tbl_19, tbl_20, tbl_21, tbl_22, tbl_23, tbl_24, tbl_25, W_top1, b_top1, W_top2, b_top2, W_top3):
    import jax
    import jax.numpy as jnp

    def _L0_rec_ref(dense_features, sparse_features):
        import jax, jax.numpy as jnp
        import numpy as np
        NUM_SPARSE = 26
        EMBED_DIM = 128
        BATCH = 2048
        F = NUM_SPARSE + 1
        combined = jnp.concatenate([dense_features[:, None, :], sparse_features], axis=1)
        interactions = jnp.einsum('bfd,bgd->bfg', combined, combined)
        iu, ju = jnp.triu_indices(F, k=1)
        interactions_flat = interactions[:, iu, ju]
        return jnp.concatenate([dense_features, interactions_flat], axis=1)
    e = jnp.stack([tbl_0[ids[:, 0]], tbl_1[ids[:, 1]], tbl_2[ids[:, 2]], tbl_3[ids[:, 3]], tbl_4[ids[:, 4]], tbl_5[ids[:, 5]], tbl_6[ids[:, 6]], tbl_7[ids[:, 7]], tbl_8[ids[:, 8]], tbl_9[ids[:, 9]], tbl_10[ids[:, 10]], tbl_11[ids[:, 11]], tbl_12[ids[:, 12]], tbl_13[ids[:, 13]], tbl_14[ids[:, 14]], tbl_15[ids[:, 15]], tbl_16[ids[:, 16]], tbl_17[ids[:, 17]], tbl_18[ids[:, 18]], tbl_19[ids[:, 19]], tbl_20[ids[:, 20]], tbl_21[ids[:, 21]], tbl_22[ids[:, 22]], tbl_23[ids[:, 23]], tbl_24[ids[:, 24]], tbl_25[ids[:, 25]]], axis=1)
    z = _L0_rec_ref(r_dense_features, e)
    z = z.reshape(z.shape[0], -1)
    h = jnp.concatenate([z, r_dense_features], axis=1)
    h = jnp.maximum(h @ W_top1 + b_top1, 0.0)
    h = jnp.maximum(h @ W_top2 + b_top2, 0.0)
    y = h @ W_top3
    return y

_drawn_inputs = setup_inputs


def setup_inputs(seed=0):
    import zlib

    import numpy as np

    out = dict(_drawn_inputs(seed))
    spreads = {'b_top1': (0.0, 0.1), 'b_top2': (0.0, 0.1)}
    factors = {}
    for name, (base, spread) in spreads.items():
        noise = np.random.default_rng([zlib.crc32(name.encode()), seed]).standard_normal(out[name].shape)
        drawn = base * np.exp(spread * noise) if base else spread * noise
        out[name] = jnp.asarray(drawn.astype(out[name].dtype))
    for name, factor in factors.items():
        out[name] = (out[name] * factor).astype(out[name].dtype)
    return out
```

```python
from contextlib import ExitStack

import concourse.bass as bass
from concourse import mybir

F32 = mybir.dt.float32
F32R = mybir.dt.float32r
I32 = mybir.dt.int32
ALU = mybir.AluOpType
ACT = mybir.ActivationFunctionType
AX = mybir.AxisListType

P = 128
SLOTS = 32

ONEHOT = [10, 11, 16, 17, 25, 26]
GROUPS = [[0, 1, 2, 3], [4, 5, 6, 7], [12, 13, 14, 15], [18, 19, 20, 21], [8, 9], [22, 23, 24]]


def dlrm_tower(nc, dense, ids, tables, w1, b1, w2, b2, w3, out):
    B, D = dense.shape
    NF = len(tables) + 1
    N1, N2 = w2.shape
    T = B // P
    NCOL = NF - 1
    NQ = (NCOL + 3) // 4
    GB = 4
    UG = 8
    UB = GB * UG
    NU = P // UB
    GC = GB * NCOL
    BK = 512
    NOH = len(ONEHOT)
    R8 = 8
    RP = tables[ONEHOT[0] - 1].shape[0] // R8
    NG = len(GROUPS)
    NPAIR = NF * (NF - 1) // 2
    ACT_CHUNKS = (3, 7)
    OHB = 4
    assert D == P and N1 == BK and sorted(sum(GROUPS, []) + ONEHOT) == list(range(NF))
    assert all(tables[f - 1].shape[0] == R8 * RP for f in ONEHOT) and w1.shape[0] == 2 * D + NPAIR

    def pair_row(i):
        return D + i * NF - i * (i + 1) // 2

    def act_stores(u, q):
        return q >= (3 if u % 2 == 0 else 2)

    with ExitStack() as ctx:
        def sb(name, shape, dt=F32):
            return ctx.enter_context(nc.sbuf_tensor(name, shape, dt))

        def sem(name):
            return ctx.enter_context(nc.semaphore(name))

        ids_i = sb("ids_i", [P, T, NF - 1], I32)
        ids_f = sb("ids_f", [P, T, NF - 1])
        ids_t = sb("ids_t", [NF - 1, T, P], F32R)
        x_rows = sb("x_rows", [P, T, D])
        rows = sb("rows", [P, 2, NF, D])
        emb_t = sb("emb_t", [P, T, P, SLOTS])
        z = sb("z", [P, 2, NQ, P])
        w_pair = sb("w_pair", [P, NQ, N1])
        w_xa = sb("w_xa", [P, N1])
        w_xb = sb("w_xb", [P, N1])
        w_x = sb("w_x", [P, N1])
        w_2 = sb("w_2", [P, N1 // P, N2])
        w_3 = sb("w_3", [P, N2])
        b_2 = sb("b_2", [1, N2])
        ones = sb("ones", [1, P])
        ident = sb("ident", [P, P])
        sel = sb("sel", [NF - 1, NOH, P], F32R)
        row_i = sb("row_i", [P, R8], I32)
        row_no = sb("row_no", [P, R8])
        neg_row = sb("neg_row", [P, R8])
        tab = sb("tab", [P, NOH, R8, D])
        tab_hi = sb("tab_hi", [P, 2, R8, D], F32R)
        tab_lo = sb("tab_lo", [P, 2, R8, D], F32R)
        hot = sb("hot", [P, OHB, B], F32R)
        away = sb("away", [P, B])
        h1 = sb("h1", [P, 2, N1])
        h1_t = sb("h1_t", [P, 2, N1 // P, P])
        h2w = sb("h2w", [P, N2])
        y = sb("y", [P, T])

        ps = ctx.enter_context(nc.psum_tensor("ps", [P, 8, BK], F32))
        TR, GRAM, H, HT = 0, 2, 6, 7
        IDV, OHA, IDA = 2, 4, 6

        ids_in = sem("ids_in")
        x_in = sem("x_in")
        tab_in = [sem(f"tab_in{n}") for n in range(NOH)]
        w_pair_in = sem("w_pair_in")
        w_x_in = sem("w_x_in")
        w_2_in = sem("w_2_in")
        small_in = sem("small_in")
        rows_in = [[sem(f"rows_in{t}_{g}") for g in range(NG)] for t in range(T)]
        y_out = sem("y_out")

        w_pair_zeroed = sem("w_pair_zeroed")
        ident_zeroed = sem("ident_zeroed")
        ident_ready = sem("ident_ready")
        row_i_ready = sem("row_i_ready")
        row_no_ready = sem("row_no_ready")
        pads_ready = sem("pads_ready")
        ids_f_ready = sem("ids_f_ready")
        ids_t_ps = sem("ids_t_ps")
        ids_t_ready = sem("ids_t_ready")
        sel_ready = sem("sel_ready")
        w_x_ready = sem("w_x_ready")
        ids_bc_dve = sem("ids_bc_dve")
        ids_bc_act = sem("ids_bc_act")
        hi_ready = sem("hi_ready")
        lo_ready = sem("lo_ready")
        hot_dve = sem("hot_dve")
        away_ready = sem("away_ready")
        hot_act = sem("hot_act")
        hot_used = sem("hot_used")
        oh_stored = sem("oh_stored")
        transposed = sem("transposed")
        stored = [sem("stored_dve"), sem("stored_act")]
        gram_ps = sem("gram_ps")
        z_dve = sem("z_dve")
        z_act = sem("z_act")
        l1_ps = sem("l1_ps")
        h1_ready = sem("h1_ready")
        h1_t_ps = sem("h1_t_ps")
        h1_t_ready = sem("h1_t_ready")
        l2_ps = sem("l2_ps")
        h2w_ready = sem("h2w_ready")
        y_ready = sem("y_ready")

        def chunks_before(n, c, on_act):
            own = [k for k in range(R8) if (k in ACT_CHUNKS) == on_act]
            return n * len(own) + sum(k <= c for k in own)

        def group_bank(t, g):
            return (t * NG + g) % 2

        def wait_all_stored(eng, t):
            for b in range(2):
                eng.wait_ge(stored[b], sum(group_bank(u, g) == b for u in range(t + 1) for g in range(NG)))

        def z_copies(t, u):
            bank = GRAM + 2 * (u % 2)
            for q in range(GB):
                for r in range(4):
                    nq = len(range(r, NCOL, 4))
                    src = ps[32 * q:32 * q + SLOTS, bank:bank + 2, 0:4 * GC].rearrange(
                        "p k (g c) -> p k g c", g=4)[:, :, :, q * NCOL + r:(q + 1) * NCOL:4]
                    dst = z[32 * r:32 * r + SLOTS, t % 2, 0:nq, u * UB:(u + 1) * UB].rearrange(
                        "p n (k g b) -> p k g n b", k=2, b=GB)[:, :, :, :, q]
                    yield q, r, src, dst

        block = ctx.enter_context(nc.Block())

        @block.sync
        def _(sp):
            sp.dma_start(ids_i[:], ids.rearrange("(t p) f -> p t f", p=P)).then_inc(ids_in, 16)
            for n, f in enumerate(ONEHOT):
                sp.dma_start(tab[0:RP, n], tables[f - 1].rearrange("(p c) d -> p c d", c=R8)).then_inc(tab_in[n], 16)
            sp.dma_start(w_xa[:], w1[0:D, :]).then_inc(w_x_in, 16)
            sp.dma_start(w_xb[:], w1[D + NPAIR:, :]).then_inc(w_x_in, 16)
            sp.wait_ge(w_pair_zeroed, 1)
            for i in range(NCOL):
                at = 32 * (i % 4)
                sp.dma_start(w_pair[at + i + 1:at + NF, i // 4, :],
                             w1[pair_row(i):pair_row(i) + NF - 1 - i, :]).then_inc(w_pair_in, 16)
            at = 32 * (NCOL % 4)
            sp.dma_start(w_pair[at:at + 1, NQ - 1, :], b1.rearrange("(a n) -> a n", a=1)).then_inc(w_pair_in, 16)
            sp.dma_start(w_2[:], w2.rearrange("(c p) n -> p c n", p=P)).then_inc(w_2_in, 16)
            sp.dma_start(b_2[:], b2.rearrange("(a n) -> a n", a=1)).then_inc(small_in, 16)
            sp.dma_start(w_3[:], w3.rearrange("n a -> a n").to_broadcast([P, N2])).then_inc(small_in, 16)
            for t in range(T):
                sp.wait_ge(y_ready, t + 1)
                sp.dma_start(out[t * P:(t + 1) * P, :], y[:, t:t + 1]).then_inc(y_out, 16)
            sp.wait_ge(y_out, 16 * T)

        @block.gpsimd
        def _(pool):
            nc.gpsimd.memset(ident[:], 0.0).then_inc(ident_zeroed, 1)
            nc.gpsimd.iota(row_i[:], pattern=[[1, R8]], base=0, channel_multiplier=R8).then_inc(row_i_ready, 1)
            pool.wait_ge(ident_zeroed, 1)
            nc.gpsimd.affine_select(out=ident[:], in_=ident[:], compare_op=ALU.not_equal, fill=1.0, base=0,
                                    pattern=[[-1, P]], channel_multiplier=1).then_inc(ident_ready, 1)
            pool.wait_ge(ids_in, 16)
            for t in range(T):
                if t >= 2:
                    pool.wait_ge(transposed, (t - 1) * NG)
                for g, feats in enumerate(GROUPS):
                    for f in feats:
                        if f:
                            pool.indirect_dma_start(
                                out=rows[:, t % 2, f, :], out_offset=None, in_=tables[f - 1],
                                in_offset=bass.IndirectOffsetOnAxis(ids_i[:, t, f - 1:f], 0),
                            ).then_inc(rows_in[t][g], 16)

        @block.scalar
        def _(act):
            act.dma_start(x_rows[:], dense.rearrange("(t p) d -> p t d", p=P)).then_inc(x_in, 16)

            def store_group(t, g):
                if group_bank(t, g) == 1:
                    f0, n = GROUPS[g][0], len(GROUPS[g])
                    act.wait_ge(transposed, t * NG + g + 1)
                    nc.scalar.copy(emb_t[:, t, :, f0:f0 + n],
                                   ps[:, TR + 1, 0:n * P].rearrange("p (f b) -> p b f", f=n)).then_inc(stored[1], 1)

            act.wait_ge(row_no_ready, 1)
            for n, f in enumerate(ONEHOT):
                act.wait_ge(tab_in[n], 16)
                if n >= 2:
                    act.wait_ge(hot_used, (n - 1) * R8)
                nc.scalar.copy(tab_hi[0:RP, n % 2], tab[0:RP, n]).then_inc(hi_ready, 1)
                act.wait_ge(ids_bc_act, n + 1)
                for c in ACT_CHUNKS:
                    k = n * R8 + c
                    a = chunks_before(n, c, True)
                    if a > 1:
                        act.wait_ge(hot_act, a - 1)
                    nc.scalar.activation(away[0:RP], ps[0:RP, IDA + n % 2, :], ACT.Abs,
                                         bias=neg_row[0:RP, c:c + 1]).then_inc(away_ready, 1)
                    act.wait_ge(away_ready, a)
                    if k >= OHB:
                        act.wait_ge(hot_used, k - OHB + 1)
                    nc.scalar.activation(hot[0:RP, k % OHB], away[0:RP], ACT.Relu, bias=1.0,
                                         scale=-1.0).then_inc(hot_act, 1)
                act.wait_ge(hot_used, (n + 1) * R8)
                nc.scalar.copy(emb_t[:, :, :, f],
                               ps[:, OHA + n % 2, :].rearrange("p (t b) -> p t b", t=T)).then_inc(oh_stored, 1)
                if n < NG:
                    store_group(0, n)

            def gram_unit(t, u):
                act.wait_ge(gram_ps, t * NU + u + 1)
                if u == 0 and t >= 2:
                    act.wait_ge(l1_ps, t - 1)
                last = None
                for q, r, src, dst in z_copies(t, u):
                    if act_stores(u, q):
                        last = nc.scalar.copy(dst, src)
                last.then_inc(z_act, 1)

            for t in range(T):
                for u in range(NU):
                    gram_unit(t, u)
                if t + 1 < T:
                    store_group(t + 1, 0)
                act.wait_ge(l1_ps, t + 1)
                nc.scalar.activation(h1[:, t % 2], ps[:, H, :], ACT.Relu).then_inc(h1_ready, 1)
                if t + 1 < T:
                    store_group(t + 1, 1)
                act.wait_ge(h1_t_ps, t + 1)
                nc.scalar.copy(h1_t[:, t % 2], ps[:, HT, :].rearrange("p (c b) -> p c b", b=P)).then_inc(h1_t_ready, 1)
                if t + 1 < T:
                    for g in range(2, NG):
                        store_group(t + 1, g)

        @block.vector
        def _(dve):
            nc.vector.memset(w_pair[:], 0.0).then_inc(w_pair_zeroed, 1)
            nc.vector.memset(ones[:], 1.0)
            nc.vector.memset(emb_t[:, :, :, NF:], 0.0)
            at = 32 * (NCOL % 4)
            nc.vector.memset(z[at:at + 1, :, NQ - 1, :], 1.0).then_inc(pads_ready, 1)
            dve.wait_ge(ids_in, 16)
            nc.vector.tensor_copy(ids_f[:], ids_i[:]).then_inc(ids_f_ready, 1)
            dve.wait_ge(row_i_ready, 1)
            nc.vector.tensor_scalar(neg_row[:], row_i[:], -1.0, None, ALU.mult)
            nc.vector.tensor_copy(row_no[:], row_i[:]).then_inc(row_no_ready, 1)
            dve.wait_ge(ident_ready, 1)
            for n, f in enumerate(ONEHOT):
                last = nc.vector.tensor_copy(sel[:, n], ident[0:NF - 1, f - 1:f].to_broadcast([NF - 1, P]))
            last.then_inc(sel_ready, 1)
            dve.wait_ge(ids_t_ps, 1)
            nc.vector.tensor_copy(ids_t[:], ps[0:NF - 1, OHA, :].rearrange("p (t b) -> p t b", t=T)).then_inc(ids_t_ready, 1)
            dve.wait_ge(row_no_ready, 1)

            def store_group(t, g):
                if group_bank(t, g) == 0:
                    f0, n = GROUPS[g][0], len(GROUPS[g])
                    dve.wait_ge(transposed, t * NG + g + 1)
                    nc.vector.tensor_copy(emb_t[:, t, :, f0:f0 + n],
                                          ps[:, TR, 0:n * P].rearrange("p (f b) -> p b f", f=n)).then_inc(stored[0], 1)

            for n in range(NOH):
                dve.wait_ge(hi_ready, n + 1)
                nc.vector.tensor_tensor(tab_lo[0:RP, n % 2], tab[0:RP, n], tab_hi[0:RP, n % 2].bitcast(F32),
                                        ALU.subtract).then_inc(lo_ready, 1)
                dve.wait_ge(ids_bc_dve, n + 1)
                for c in range(R8):
                    if c not in ACT_CHUNKS:
                        k = n * R8 + c
                        if k >= OHB:
                            dve.wait_ge(hot_used, k - OHB + 1)
                        nc.vector.tensor_scalar(hot[0:RP, k % OHB], ps[0:RP, IDV + n % 2, :], row_no[0:RP, c:c + 1],
                                                None, ALU.is_equal).then_inc(hot_dve, 1)
                if n < NG:
                    store_group(0, n)
            dve.wait_ge(w_x_in, 32)
            nc.vector.tensor_tensor(w_x[:], w_xa[:], w_xb[:], ALU.add).then_inc(w_x_ready, 1)

            for t in range(T):
                for u in range(NU):
                    dve.wait_ge(gram_ps, t * NU + u + 1)
                    if u == 0 and t >= 2:
                        dve.wait_ge(l1_ps, t - 1)
                    last = None
                    for q, r, src, dst in z_copies(t, u):
                        if not act_stores(u, q):
                            last = nc.vector.tensor_copy(dst, src)
                    last.then_inc(z_dve, 1)
                if t + 1 < T:
                    for g in range(NG - 1):
                        store_group(t + 1, g)
                dve.wait_ge(l2_ps, t + 1)
                if t == 0:
                    dve.wait_ge(small_in, 32)
                if t >= 1:
                    dve.wait_ge(y_ready, t)
                nc.vector.scalar_tensor_tensor(out=h2w[:], in0=ps[:, H, 0:N2], scalar=0.0, in1=w_3[:],
                                               op0=ALU.max, op1=ALU.mult).then_inc(h2w_ready, 1)
                dve.wait_ge(h2w_ready, t + 1)
                nc.vector.tensor_reduce(out=y[:, t:t + 1], in_=h2w[:], axis=AX.X, op=ALU.add).then_inc(y_ready, 1)
                if t + 1 < T:
                    store_group(t + 1, NG - 1)

        @block.tensor
        def _(pe):
            pe.wait_ge(ids_f_ready, 1)
            pe.wait_ge(ident_ready, 1)
            for t in range(T):
                last = nc.tensor.transpose(ps[0:NF - 1, OHA, t * P:(t + 1) * P], ids_f[:, t], ident[:])
            last.then_inc(ids_t_ps, 1)

            def broadcast_ids(n):
                if n >= 2:
                    pe.wait_ge(hot_dve, chunks_before(n - 2, R8 - 1, False))
                nc.tensor.matmul(ps[:, IDV + n % 2, :], sel[:, n], ids_t[:].rearrange("p t b -> p (t b)"),
                                 start=True, stop=True).then_inc(ids_bc_dve, 1)
                if n >= 2:
                    pe.wait_ge(hot_act, chunks_before(n - 2, R8 - 1, True))
                nc.tensor.matmul(ps[:, IDA + n % 2, :], sel[:, n], ids_t[:].rearrange("p t b -> p (t b)"),
                                 start=True, stop=True).then_inc(ids_bc_act, 1)

            def transpose_group(t, g):
                k = t * NG + g
                feats = GROUPS[g]
                if 0 in feats:
                    pe.wait_ge(x_in, 16)
                pe.wait_ge(rows_in[t][g], 16 * (len(feats) - (0 in feats)))
                if k >= 2:
                    pe.wait_ge(stored[k % 2], k // 2)
                for m, f in enumerate(feats):
                    src = rows[:, t % 2, f, :] if f else x_rows[:, t]
                    last = nc.tensor.transpose(ps[:, TR + k % 2, m * P:(m + 1) * P], src, ident[:])
                last.then_inc(transposed, 1)

            pe.wait_ge(sel_ready, 1)
            pe.wait_ge(ids_t_ready, 1)
            broadcast_ids(0)
            for n in range(NOH):
                if n + 1 < NOH:
                    broadcast_ids(n + 1)
                pe.wait_ge(hi_ready, n + 1)
                pe.wait_ge(lo_ready, n + 1)
                if n >= 2:
                    pe.wait_ge(oh_stored, n - 1)
                for c in range(R8):
                    k = n * R8 + c
                    on_act = c in ACT_CHUNKS
                    pe.wait_ge(hot_act if on_act else hot_dve, chunks_before(n, c, on_act))
                    nc.tensor.matmul(ps[:, OHA + n % 2, :], tab_hi[0:RP, n % 2, c], hot[0:RP, k % OHB],
                                     start=c == 0, stop=False)
                    last = nc.tensor.matmul(ps[:, OHA + n % 2, :], tab_lo[0:RP, n % 2, c], hot[0:RP, k % OHB],
                                            start=False, stop=c == R8 - 1)
                    last.then_inc(hot_used, 1)
                if n < NG:
                    transpose_group(0, n)

            def gram_unit(t, u):
                k = t * NU + u
                if k >= 2:
                    pe.wait_ge(z_dve, k - 1)
                    pe.wait_ge(z_act, k - 1)
                for g in range(UG):
                    b0 = u * UB + g * GB
                    last = nc.tensor.matmul(ps[:, GRAM + 2 * (u % 2) + g // 4, g % 4 * GC:(g % 4 + 1) * GC],
                                            emb_t[:, t, b0:b0 + GB, :].rearrange("p b f -> p (b f)"),
                                            emb_t[:, t, b0:b0 + GB, 0:NCOL], start=True, stop=True)
                last.then_inc(gram_ps, 1)

            def layer1(t):
                if t == 0:
                    pe.wait_ge(w_x_ready, 1)
                    pe.wait_ge(w_pair_in, 16 * (NCOL + 1))
                else:
                    pe.wait_ge(h2w_ready, t)
                nc.tensor.matmul(ps[:, H, :], emb_t[:, t, :, 0], w_x[:], start=True, stop=False)
                pe.wait_ge(z_dve, (t + 1) * NU)
                pe.wait_ge(z_act, (t + 1) * NU)
                for k in range(NQ):
                    rows_used = P if k < NQ - 1 else 32 * (NCOL % 4) + 1
                    last = nc.tensor.matmul(ps[:, H, :], z[0:rows_used, t % 2, k, :], w_pair[0:rows_used, k, :],
                                            start=False, stop=k == NQ - 1)
                last.then_inc(l1_ps, 1)

            def transpose_h1(t):
                pe.wait_ge(h1_ready, t + 1)
                if t >= 1:
                    pe.wait_ge(h1_t_ready, t)
                for c in range(N1 // P):
                    last = nc.tensor.transpose(ps[:, HT, c * P:(c + 1) * P], h1[:, t % 2, c * P:(c + 1) * P], ident[:])
                last.then_inc(h1_t_ps, 1)

            def layer2(t):
                pe.wait_ge(h1_t_ready, t + 1)
                if t == 0:
                    pe.wait_ge(w_2_in, 16)
                    pe.wait_ge(small_in, 32)
                for c in range(N1 // P):
                    nc.tensor.matmul(ps[:, H, 0:N2], h1_t[:, t % 2, c], w_2[:, c], start=c == 0, stop=False)
                nc.tensor.matmul(ps[:, H, 0:N2], ones[0:1, :], b_2[0:1, :], start=False, stop=True).then_inc(l2_ps, 1)

            pe.wait_ge(pads_ready, 1)
            for t in range(T):
                wait_all_stored(pe, t)
                if t == 0:
                    pe.wait_ge(oh_stored, NOH)
                for u in range(NU):
                    gram_unit(t, u)
                if t + 1 < T:
                    transpose_group(t + 1, 0)
                layer1(t)
                if t + 1 < T:
                    transpose_group(t + 1, 1)
                transpose_h1(t)
                if t + 1 < T:
                    for g in range(2, NG - 1):
                        transpose_group(t + 1, g)
                layer2(t)
                if t + 1 < T:
                    transpose_group(t + 1, NG - 1)


def kernel(**inputs):
    import numpy as _np
    import concourse.bacc as _bacc
    from concourse import mybir as _mybir
    from concourse.bass_utils import run_bass_kernel_spmd as _run

    nc = _bacc.Bacc("TRN2", target_bir_lowering=False, num_devices=1)
    arrays, aps = {}, {}
    tables = [f"tbl_{n}" for n in range(26)]
    for name in ["r_dense_features", "ids", *tables, "W_top1", "b_top1", "W_top2", "b_top2", "W_top3"]:
        a = _np.ascontiguousarray(inputs[name])
        arrays[f"in_{name}_dram"] = a
        aps[name] = nc.dram_tensor(f"in_{name}_dram", a.shape, _mybir.dt.from_np(a.dtype), kind="ExternalInput").ap()
    out = nc.dram_tensor("out_dram", (inputs["r_dense_features"].shape[0], 1), F32, kind="ExternalOutput").ap()
    dlrm_tower(nc, aps["r_dense_features"], aps["ids"], [aps[n] for n in tables], aps["W_top1"], aps["b_top1"],
               aps["W_top2"], aps["b_top2"], aps["W_top3"], out)
    r = _run(nc, [arrays], core_ids=[0])
    return r.results[0]["out_dram"]
```

```python
from contextlib import ExitStack

import concourse.bass as bass
from concourse import mybir

F32 = mybir.dt.float32
F32R = mybir.dt.float32r
I32 = mybir.dt.int32
ALU = mybir.AluOpType
ACT = mybir.ActivationFunctionType
AX = mybir.AxisListType

P = 128
SLOTS = 32

ONEHOT = [10, 11, 16, 17, 18]
GROUPS = [[(0, 4)], [(4, 4)], [(12, 4)], [(19, 4)], [(23, 4)], [(8, 2)]]


def features(group):
    return [f + k for f, n in group for k in range(n)]


def plan_steps(T, NU, NOH, NG, ND):
    steps = []
    for n in range(NOH):
        steps.append(("hot", 0, n))
        if 1 <= n <= NG:
            steps.append(("group", 0, n - 1))
    steps += [("group", 0, g) for g in range(NOH - 1, NG)]
    later = [("hot", 1, n) for n in range(NOH)]
    for t in range(T):
        chains = [c for c in ((t - 1,) if t <= ND else ()) if c >= 0] + ([t] if t >= ND else [])
        fill = [later.pop(0) for _ in range(min(len(later), (NOH + 1) // 2))]
        groups = [("group", t + 1, g) for g in range(NG)] if t + 1 < T else []
        for u in range(NU):
            steps.append(("gram", t, u))
            if u in (0, 2) and fill:
                steps.append(fill.pop(0))
        for c in chains:
            steps += groups[:1] + [("l1", c)]
            steps += groups[1:2] + [("h1", c)]
            steps += (fill[:1] or groups[2:3]) + [("l2", c)]
            groups = groups[2:] if fill else groups[3:]
            fill = fill[1:]
        steps += groups[:3] + fill + groups[3:]
    return steps


def dlrm_tower(nc, dense, ids, tables, w1, b1, w2, b2, w3, out):
    B, D = dense.shape
    NF = len(tables) + 1
    N1, N2 = w2.shape
    T = B // P
    HT = T // 2
    HB = HT * P
    NCOL = NF - 1
    NQ = (NCOL + 3) // 4
    GB = 4
    UG = 8
    UB = GB * UG
    NU = P // UB
    GC = GB * NCOL
    BK = 512
    NOH = len(ONEHOT)
    R8 = 8
    RP = tables[ONEHOT[0] - 1].shape[0] // R8
    NG = len(GROUPS)
    NPAIR = NF * (NF - 1) // 2
    ND = 2
    ACT_CHUNKS = (2, 4, 7)
    OHB = 16
    RAW = 2
    gathered = [f for g in GROUPS for f in features(g) if f]
    assert D == P and N1 == BK and sorted(gathered + ONEHOT) == list(range(1, NF))
    assert all(tables[f - 1].shape[0] == R8 * RP for f in ONEHOT) and w1.shape[0] == 2 * D + NPAIR

    steps = plan_steps(T, NU, NOH, NG, ND)
    banked = [s for s in steps if s[0] in ("hot", "group", "h1")]

    def bank_of(s):
        return banked.index(s) % 2

    def stored_by_act(s):
        return s[0] != "group" or s[2] % 2 == 1

    def stored_count(s):
        return sum(stored_by_act(b) == stored_by_act(s) for b in banked[:banked.index(s) + 1])

    def pair_row(i):
        return D + i * NF - i * (i + 1) // 2

    def pair_runs():
        for i in range(NCOL):
            n, j = pair_row(i) - D, i + 1
            while j < NF:
                k = min(NF - j, P - n % P)
                yield i, j, k, n // P, n % P
                n, j = n + k, j + k

    PACKS = len(list(pair_runs()))
    NK = NPAIR // P + 1
    KR = NPAIR - (NK - 1) * P
    assert 64 <= KR < 96

    def act_stores(t, q):
        return q >= (1 if t < 2 else 2)

    def act_builds(h, c):
        return h == 0 and c in ACT_CHUNKS

    def chunks_built(h, n, c, on_act):
        return sum(act_builds(a, k) == on_act
                   for a in range(h + 1) for m in range(NOH if a < h else n + 1)
                   for k in range(R8 if (a, m) != (h, n) else c + 1))

    def next_hot(s):
        m = s[1] * NOH + s[2] + 1
        return (m // NOH, m % NOH) if m < 2 * NOH else None

    def chunk_no(h, n, c):
        return (h * NOH + n) * R8 + c

    with ExitStack() as ctx:
        def sb(name, shape, dt=F32):
            return ctx.enter_context(nc.sbuf_tensor(name, shape, dt))

        def sem(name):
            return ctx.enter_context(nc.semaphore(name))

        ids_i = sb("ids_i", [P, T, NF - 1], I32)
        ids_f = sb("ids_f", [P, T, NF - 1])
        ids_t = sb("ids_t", [NF - 1, B], F32R)
        x_rows = sb("x_rows", [P, T, D])
        rows = sb("rows", [P, 2, len(gathered), D])
        emb_t = sb("emb_t", [P, T, P, SLOTS])
        z = sb("z", [P, 2, NQ, P])
        w_pair = sb("w_pair", [P, NQ, N1])
        zd = sb("zd", [P, 2, NK, P])
        w_d = sb("w_d", [P, NK, N1])
        w_x = sb("w_x", [P, N1])
        w_2 = sb("w_2", [P, N1 // P, N2])
        w_3 = sb("w_3", [P, N2])
        b_2 = sb("b_2", [1, N2])
        ones = sb("ones", [1, P])
        zeros = sb("zeros", [P, 1])
        ident = sb("ident", [P, P])
        ident_r = sb("ident_r", [NF - 1, NF - 1], F32R)
        row_i = sb("row_i", [P, R8], I32)
        row_no = sb("row_no", [P, R8])
        neg_row = sb("neg_row", [P, R8])
        tab = sb("tab", [P, RAW, R8, D])
        tab_hi = sb("tab_hi", [P, NOH, R8, D], F32R)
        tab_lo = sb("tab_lo", [P, NOH, R8, D], F32R)
        hot = sb("hot", [P, OHB, HB], F32R)
        away = sb("away", [P, 2, HB])
        h1 = sb("h1", [P, N1])
        w_xb = h1
        h1_t = sb("h1_t", [P, N1 // P, P])
        h2w = sb("h2w", [P, N2])
        y = sb("y", [P, T])

        ps = ctx.enter_context(nc.psum_tensor("ps", [P, 8, BK], F32))
        ROT, GRAM, H, IDS = 0, 2, 6, 7
        IDV, IDA = 2, 4

        ids_in = sem("ids_in")
        x_in = sem("x_in")
        tab_in = [sem(f"tab_in{n}") for n in range(NOH)]
        w_pair_in = sem("w_pair_in")
        w_d_in = sem("w_d_in")
        zd_in = [sem(f"zd_in{t}") for t in range(ND)]
        w_x_in = sem("w_x_in")
        w_2_in = sem("w_2_in")
        small_in = sem("small_in")
        rows_in = [[sem(f"rows_in{t}_{g}") for g in range(NG)] for t in range(T)]
        y_out = sem("y_out")

        zeros_ready = sem("zeros_ready")
        w_pair_zeroed = sem("w_pair_zeroed")
        ident_zeroed = sem("ident_zeroed")
        ident_ready = sem("ident_ready")
        row_i_ready = sem("row_i_ready")
        row_no_ready = sem("row_no_ready")
        pads_ready = sem("pads_ready")
        ids_f_ready = sem("ids_f_ready")
        ids_t_ps = sem("ids_t_ps")
        ids_t_ready = sem("ids_t_ready")
        w_x_ready = sem("w_x_ready")
        ids_bc_dve = sem("ids_bc_dve")
        ids_bc_act = sem("ids_bc_act")
        hi_ready = sem("hi_ready")
        lo_ready = sem("lo_ready")
        hot_dve = sem("hot_dve")
        away_ready = sem("away_ready")
        hot_act = sem("hot_act")
        hot_used = sem("hot_used")
        group_ps = sem("group_ps")
        stored_dve = sem("stored_dve")
        stored_act = sem("stored_act")
        gram_ps = sem("gram_ps")
        z_dve = sem("z_dve")
        z_act = sem("z_act")
        l1_ps = sem("l1_ps")
        h1_ready = sem("h1_ready")
        h1_t_ps = sem("h1_t_ps")
        l2_ps = sem("l2_ps")
        h2w_ready = sem("h2w_ready")
        y_ready = sem("y_ready")

        def wait_stored(eng, s):
            eng.wait_ge(stored_act if stored_by_act(s) else stored_dve, stored_count(s))

        def wait_z_free(eng, t):
            if t - 2 < ND:
                eng.wait_ge(zd_in[t - 2], 16 * PACKS)
            else:
                eng.wait_ge(l1_ps, t - 1)

        def z_copies(t, u):
            bank = GRAM + 2 * (u % 2)
            for q in range(GB):
                for r in range(4):
                    nq = len(range(r, NCOL, 4))
                    src = ps[32 * q:32 * q + SLOTS, bank:bank + 2, 0:4 * GC].rearrange(
                        "p k (g c) -> p k g c", g=4)[:, :, :, q * NCOL + r:(q + 1) * NCOL:4]
                    dst = z[32 * r:32 * r + SLOTS, t % 2, 0:nq, u * UB:(u + 1) * UB].rearrange(
                        "p n (k g b) -> p k g b n", k=2, b=GB)[:, :, :, q, :]
                    yield q, src, dst

        def group_copies(s):
            _, t, g = s
            m = 0
            for f0, n in GROUPS[g]:
                yield (emb_t[:, t, :, f0:f0 + n],
                       ps[:, ROT + bank_of(s), m * P:(m + n) * P].rearrange("p (f b) -> p b f", f=n))
                m += n

        block = ctx.enter_context(nc.Block())

        @block.sync
        def _(sp):
            sp.dma_start(ids_i[:], ids.rearrange("(t p) f -> p t f", p=P)).then_inc(ids_in, 16)
            for n, f in enumerate(ONEHOT):
                if n >= RAW:
                    sp.wait_ge(lo_ready, n - RAW + 1)
                sp.dma_start(tab[0:RP, n % RAW], tables[f - 1].rearrange("(p c) d -> p c d", c=R8)).then_inc(tab_in[n], 16)
            sp.dma_start(w_x[:], w1[0:D, :]).then_inc(w_x_in, 16)
            sp.dma_start(w_xb[:], w1[D + NPAIR:, :]).then_inc(w_x_in, 16)
            sp.dma_start(w_d[:, 0:NK - 1, :], w1[D:D + (NK - 1) * P, :].rearrange("(k p) n -> p k n", p=P)).then_inc(w_d_in, 16)
            sp.dma_start(w_d[0:KR, NK - 1, :], w1[D + (NK - 1) * P:D + NPAIR, :]).then_inc(w_d_in, 16)
            sp.dma_start(w_d[KR:KR + 1, NK - 1, :], b1.rearrange("(a n) -> a n", a=1)).then_inc(w_d_in, 16)
            sp.dma_start(w_2[:], w2.rearrange("(c p) n -> p c n", p=P)).then_inc(w_2_in, 16)
            sp.dma_start(b_2[:], b2.rearrange("(a n) -> a n", a=1)).then_inc(small_in, 16)
            sp.dma_start(w_3[:], w3.rearrange("n a -> a n").to_broadcast([P, N2])).then_inc(small_in, 16)
            sp.wait_ge(w_pair_zeroed, 1)
            for i in range(NCOL):
                at = 32 * (i % 4)
                sp.dma_start(w_pair[at + i + 1:at + NF, i // 4, :],
                             w1[pair_row(i):pair_row(i) + NF - 1 - i, :]).then_inc(w_pair_in, 16)
            at = 32 * (NCOL % 4)
            sp.dma_start(w_pair[at:at + 1, NQ - 1, :], b1.rearrange("(a n) -> a n", a=1)).then_inc(w_pair_in, 16)
            sp.wait_ge(pads_ready, 1)
            for t in range(ND):
                sp.wait_ge(z_dve, (t + 1) * NU)
                sp.wait_ge(z_act, (t + 1) * NU)
                for i, j, n, k, p in pair_runs():
                    at = 32 * (i % 4) + j
                    sp.dma_start(zd[p:p + n, t % 2, k, :], z[at:at + n, t % 2, i // 4, :]).then_inc(zd_in[t], 16)
            for t in range(T):
                sp.wait_ge(y_ready, t + 1)
                sp.dma_start(out[t * P:(t + 1) * P, :], y[:, t:t + 1]).then_inc(y_out, 16)
            sp.wait_ge(y_out, 16 * T)

        @block.gpsimd
        def _(pool):
            nc.gpsimd.memset(ident[:], 0.0).then_inc(ident_zeroed, 1)
            nc.gpsimd.iota(row_i[:], pattern=[[1, R8]], base=0, channel_multiplier=R8).then_inc(row_i_ready, 1)
            pool.wait_ge(ident_zeroed, 1)
            nc.gpsimd.affine_select(out=ident[:], in_=ident[:], compare_op=ALU.not_equal, fill=1.0, base=0,
                                    pattern=[[-1, P]], channel_multiplier=1).then_inc(ident_ready, 1)
            pool.wait_ge(ids_in, 16)
            for t in range(T):
                if t >= 2:
                    pool.wait_ge(group_ps, (t - 1) * NG)
                for g, group in enumerate(GROUPS):
                    for f in features(group):
                        if f:
                            pool.indirect_dma_start(
                                out=rows[:, t % 2, gathered.index(f), :], out_offset=None, in_=tables[f - 1],
                                in_offset=bass.IndirectOffsetOnAxis(ids_i[:, t, f - 1:f], 0),
                            ).then_inc(rows_in[t][g], 16)

        @block.scalar
        def _(act):
            act.dma_start(x_rows[:], dense.rearrange("(t p) d -> p t d", p=P)).then_inc(x_in, 16)
            act.wait_ge(zeros_ready, 1)
            nc.scalar.copy(w_pair[:].rearrange("p k n -> p (k n)"),
                           zeros[:].to_broadcast([P, NQ * N1])).then_inc(w_pair_zeroed, 1)

            def split_hi(n):
                act.wait_ge(tab_in[n], 16)
                nc.scalar.copy(tab_hi[0:RP, n], tab[0:RP, n % RAW]).then_inc(hi_ready, 1)

            def build_hots(h, n):
                act.wait_ge(ids_bc_act, n + 1)

                def one_hot(c):
                    a = chunks_built(h, n, c, True)
                    act.wait_ge(away_ready, a)
                    k = chunk_no(h, n, c)
                    if k >= OHB:
                        act.wait_ge(hot_used, k - OHB + 1)
                    nc.scalar.activation(hot[0:RP, k % OHB], away[0:RP, a % 2], ACT.Relu, bias=1.0,
                                         scale=-1.0).then_inc(hot_act, 1)

                for m, c in enumerate(ACT_CHUNKS):
                    a = chunks_built(h, n, c, True)
                    if a == 1:
                        act.wait_ge(row_no_ready, 1)
                    if a > 2:
                        act.wait_ge(hot_act, a - 2)
                    nc.scalar.activation(away[0:RP, a % 2], ps[0:RP, IDA + n % 2, 0:HB], ACT.Abs,
                                         bias=neg_row[0:RP, c:c + 1]).then_inc(away_ready, 1)
                    if m:
                        one_hot(ACT_CHUNKS[m - 1])
                one_hot(ACT_CHUNKS[-1])

            def store_hot(s):
                _, h, n = s
                act.wait_ge(hot_used, chunk_no(h, n, R8 - 1) + 1)
                nc.scalar.copy(emb_t[:, h * HT:(h + 1) * HT, :, ONEHOT[n]],
                               ps[:, ROT + bank_of(s), 0:HB].rearrange("p (t b) -> p t b", t=HT)).then_inc(stored_act, 1)

            split_hi(0)
            build_hots(0, 0)
            split_hi(1)
            for s in steps:
                if s[0] == "hot":
                    ahead = next_hot(s)
                    if ahead and ahead[0] == 0:
                        build_hots(*ahead)
                        if ahead[1] + 1 < NOH:
                            split_hi(ahead[1] + 1)
                    store_hot(s)
                if s[0] == "group" and stored_by_act(s):
                    act.wait_ge(group_ps, s[1] * NG + s[2] + 1)
                    copies = list(group_copies(s))
                    for dst, src in copies[:-1]:
                        nc.scalar.copy(dst, src)
                    nc.scalar.copy(*copies[-1]).then_inc(stored_act, 1)
                elif s[0] == "gram":
                    _, t, u = s
                    act.wait_ge(gram_ps, t * NU + u + 1)
                    if u == 0 and t >= 2:
                        wait_z_free(act, t)
                    last = None
                    for q, src, dst in z_copies(t, u):
                        if act_stores(t, q):
                            last = nc.scalar.copy(dst, src)
                    last.then_inc(z_act, 1)
                elif s[0] == "l1":
                    t = s[1]
                    act.wait_ge(l1_ps, t + 1)
                    if t >= 1:
                        act.wait_ge(h1_t_ps, t)
                    nc.scalar.activation(h1[:], ps[:, H, :], ACT.Relu).then_inc(h1_ready, 1)
                elif s[0] == "h1":
                    t = s[1]
                    act.wait_ge(h1_t_ps, t + 1)
                    if t >= 1:
                        act.wait_ge(l2_ps, t)
                    nc.scalar.copy(h1_t[:], ps[:, ROT + bank_of(s), :].rearrange(
                        "p (c b) -> p c b", b=P)).then_inc(stored_act, 1)

        @block.vector
        def _(dve):
            nc.vector.memset(zeros[:], 0.0).then_inc(zeros_ready, 1)
            nc.vector.memset(ones[:], 1.0)
            nc.vector.memset(emb_t[:, 0:HT, :, NF:], 0.0)
            dve.wait_ge(ids_in, 16)
            nc.vector.tensor_copy(ids_f[:], ids_i[:]).then_inc(ids_f_ready, 1)
            dve.wait_ge(ident_ready, 1)
            nc.vector.tensor_copy(ident_r[:], ident[0:NF - 1, 0:NF - 1])
            dve.wait_ge(row_i_ready, 1)
            nc.vector.tensor_scalar(neg_row[:], row_i[:], -1.0, None, ALU.mult)
            nc.vector.tensor_copy(row_no[:], row_i[:]).then_inc(row_no_ready, 1)
            dve.wait_ge(ids_t_ps, 1)
            nc.vector.tensor_copy(ids_t[:], ps[0:NF - 1, IDS, :]).then_inc(ids_t_ready, 1)
            dve.wait_ge(row_no_ready, 1)

            def build_hots(h, n):
                dve.wait_ge(ids_bc_dve, h * NOH + n + 1)
                for c in range(R8):
                    if h == 0 and c == 3:
                        dve.wait_ge(hi_ready, n + 1)
                        nc.vector.tensor_tensor(tab_lo[0:RP, n], tab[0:RP, n % RAW], tab_hi[0:RP, n].bitcast(F32),
                                                ALU.subtract).then_inc(lo_ready, 1)
                    if not act_builds(h, c):
                        k = chunk_no(h, n, c)
                        if k >= OHB:
                            dve.wait_ge(hot_used, k - OHB + 1)
                        bank = IDV + n % 2 if h == 0 else IDS
                        nc.vector.tensor_scalar(hot[0:RP, k % OHB], ps[0:RP, bank, 0:HB], row_no[0:RP, c:c + 1],
                                                None, ALU.is_equal).then_inc(hot_dve, 1)

            build_hots(0, 0)
            nc.vector.memset(emb_t[:, HT:, :, NF:], 0.0)
            at = 32 * (NCOL % 4)
            nc.vector.memset(z[at:at + 1, :, NQ - 1, :], 1.0)
            nc.vector.memset(zd[64:KR + 1, :, NK - 1, :], 1.0).then_inc(pads_ready, 1)
            for s in steps:
                if s[0] == "hot":
                    if next_hot(s):
                        build_hots(*next_hot(s))
                elif s[0] == "group" and not stored_by_act(s):
                    dve.wait_ge(group_ps, s[1] * NG + s[2] + 1)
                    copies = list(group_copies(s))
                    for dst, src in copies[:-1]:
                        nc.vector.tensor_copy(dst, src)
                    nc.vector.tensor_copy(*copies[-1]).then_inc(stored_dve, 1)
                elif s[0] == "gram":
                    _, t, u = s
                    if (t, u) == (0, 0):
                        dve.wait_ge(w_x_in, 32)
                        nc.vector.tensor_tensor(w_x[:], w_x[:], w_xb[:], ALU.add).then_inc(w_x_ready, 1)
                    dve.wait_ge(gram_ps, t * NU + u + 1)
                    if u == 0 and t >= 2:
                        wait_z_free(dve, t)
                    last = None
                    for q, src, dst in z_copies(t, u):
                        if not act_stores(t, q):
                            last = nc.vector.tensor_copy(dst, src)
                    last.then_inc(z_dve, 1)
                elif s[0] == "l2":
                    t = s[1]
                    dve.wait_ge(l2_ps, t + 1)
                    if t == 0:
                        dve.wait_ge(small_in, 32)
                    if t >= 1:
                        dve.wait_ge(y_ready, t)
                    nc.vector.scalar_tensor_tensor(out=h2w[:], in0=ps[:, H, 0:N2], scalar=0.0, in1=w_3[:],
                                                   op0=ALU.max, op1=ALU.mult).then_inc(h2w_ready, 1)
                    dve.wait_ge(h2w_ready, t + 1)
                    nc.vector.tensor_reduce(out=y[:, t:t + 1], in_=h2w[:], axis=AX.X, op=ALU.add).then_inc(y_ready, 1)

        @block.tensor
        def _(pe):
            pe.wait_ge(ids_f_ready, 1)
            pe.wait_ge(ident_ready, 1)
            for t in range(T):
                last = nc.tensor.transpose(ps[0:NF - 1, IDS, t * P:(t + 1) * P], ids_f[:, t], ident[:])
            last.then_inc(ids_t_ps, 1)

            def broadcast_ids(h, n):
                f = ONEHOT[n] - 1
                picks = ident_r[:, f:f + 1].to_broadcast([NF - 1, P])
                if h == 0:
                    if n >= 2:
                        pe.wait_ge(hot_dve, chunks_built(0, n - 2, R8 - 1, False))
                        pe.wait_ge(hot_act, chunks_built(0, n - 2, R8 - 1, True))
                    nc.tensor.matmul(ps[:, IDV + n % 2, 0:HB], picks, ids_t[:, 0:HB],
                                     start=True, stop=True).then_inc(ids_bc_dve, 1)
                    nc.tensor.matmul(ps[:, IDA + n % 2, 0:HB], picks, ids_t[:, 0:HB],
                                     start=True, stop=True).then_inc(ids_bc_act, 1)
                else:
                    if n >= 1:
                        pe.wait_ge(hot_dve, chunks_built(1, n - 1, R8 - 1, False))
                    nc.tensor.matmul(ps[:, IDS, 0:HB], picks, ids_t[:, HB:2 * HB],
                                     start=True, stop=True).then_inc(ids_bc_dve, 1)

            def wait_bank(s):
                k = banked.index(s)
                if k >= 2:
                    wait_stored(pe, banked[k - 2])

            pe.wait_ge(ids_t_ready, 1)
            broadcast_ids(0, 0)
            broadcast_ids(0, 1)
            for s in steps:
                if s[0] == "hot":
                    _, h, n = s
                    if h == 1 and n + 1 < NOH:
                        broadcast_ids(1, n + 1)
                    wait_bank(s)
                    if h == 0:
                        pe.wait_ge(hi_ready, n + 1)
                    bank = ps[:, ROT + bank_of(s), 0:HB]
                    for c in range(R8):
                        on_act = act_builds(h, c)
                        pe.wait_ge(hot_act if on_act else hot_dve, chunks_built(h, n, c, on_act))
                        one_hot = hot[0:RP, chunk_no(h, n, c) % OHB]
                        nc.tensor.matmul(bank, tab_hi[0:RP, n, c], one_hot, start=c == 0, stop=False)
                        if h == 0 and c == 0:
                            pe.wait_ge(lo_ready, n + 1)
                        nc.tensor.matmul(bank, tab_lo[0:RP, n, c], one_hot,
                                         start=False, stop=c == R8 - 1).then_inc(hot_used, 1)
                    if h == 0:
                        if n + 2 < NOH:
                            broadcast_ids(0, n + 2)
                        elif n + 2 == NOH:
                            broadcast_ids(1, 0)
                elif s[0] == "group":
                    _, t, g = s
                    feats = features(GROUPS[g])
                    if 0 in feats:
                        pe.wait_ge(x_in, 16)
                    pe.wait_ge(rows_in[t][g], 16 * (len(feats) - (0 in feats)))
                    wait_bank(s)
                    for m, f in enumerate(feats):
                        src = rows[:, t % 2, gathered.index(f), :] if f else x_rows[:, t]
                        last = nc.tensor.transpose(ps[:, ROT + bank_of(s), m * P:(m + 1) * P], src, ident[:])
                    last.then_inc(group_ps, 1)
                elif s[0] == "gram":
                    _, t, u = s
                    if u == 0:
                        if t == 0:
                            pe.wait_ge(pads_ready, 1)
                        for b in [("group", t, g) for g in range(NG)] + [("hot", t // HT, NOH - 1)]:
                            wait_stored(pe, b)
                        if t == 0:
                            pe.wait_ge(hot_dve, chunks_built(0, NOH - 1, R8 - 1, False))
                            pe.wait_ge(hot_act, chunks_built(0, NOH - 1, R8 - 1, True))
                    k = t * NU + u
                    if k >= 2:
                        pe.wait_ge(z_dve, k - 1)
                        pe.wait_ge(z_act, k - 1)
                    for g in range(UG):
                        b0 = u * UB + g * GB
                        last = nc.tensor.matmul(ps[:, GRAM + 2 * (u % 2) + g // 4, g % 4 * GC:(g % 4 + 1) * GC],
                                                emb_t[:, t, b0:b0 + GB, :].rearrange("p b f -> p (b f)"),
                                                emb_t[:, t, b0:b0 + GB, 0:NCOL], start=True, stop=True)
                    last.then_inc(gram_ps, 1)
                elif s[0] == "l1":
                    t = s[1]
                    if t == 0:
                        pe.wait_ge(w_x_ready, 1)
                        pe.wait_ge(w_d_in, 48)
                    else:
                        pe.wait_ge(h2w_ready, t)
                    nc.tensor.matmul(ps[:, H, :], emb_t[:, t, :, 0], w_x[:], start=True, stop=False)
                    if t < ND:
                        pe.wait_ge(zd_in[t], 16 * PACKS)
                        for k in range(NK):
                            used = P if k < NK - 1 else KR + 1
                            last = nc.tensor.matmul(ps[:, H, :], zd[0:used, t % 2, k, :], w_d[0:used, k, :],
                                                    start=False, stop=k == NK - 1)
                    else:
                        if t == ND:
                            pe.wait_ge(w_pair_in, 16 * (NCOL + 1))
                        pe.wait_ge(z_dve, (t + 1) * NU)
                        pe.wait_ge(z_act, (t + 1) * NU)
                        for k in range(NQ):
                            used = P if k < NQ - 1 else 32 * (NCOL % 4) + 1
                            last = nc.tensor.matmul(ps[:, H, :], z[0:used, t % 2, k, :], w_pair[0:used, k, :],
                                                    start=False, stop=k == NQ - 1)
                    last.then_inc(l1_ps, 1)
                elif s[0] == "h1":
                    t = s[1]
                    pe.wait_ge(h1_ready, t + 1)
                    wait_bank(s)
                    for c in range(N1 // P):
                        last = nc.tensor.transpose(ps[:, ROT + bank_of(s), c * P:(c + 1) * P],
                                                   h1[:, c * P:(c + 1) * P], ident[:])
                    last.then_inc(h1_t_ps, 1)
                elif s[0] == "l2":
                    t = s[1]
                    wait_stored(pe, ("h1", t))
                    if t == 0:
                        pe.wait_ge(w_2_in, 16)
                        pe.wait_ge(small_in, 32)
                    for c in range(N1 // P):
                        nc.tensor.matmul(ps[:, H, 0:N2], h1_t[:, c], w_2[:, c], start=c == 0, stop=False)
                    nc.tensor.matmul(ps[:, H, 0:N2], ones[0:1, :], b_2[0:1, :],
                                     start=False, stop=True).then_inc(l2_ps, 1)


def kernel(**inputs):
    import numpy as _np
    import concourse.bacc as _bacc
    from concourse import mybir as _mybir
    from concourse.bass_utils import run_bass_kernel_spmd as _run

    nc = _bacc.Bacc("TRN2", target_bir_lowering=False, num_devices=1)
    arrays, aps = {}, {}
    tables = [f"tbl_{n}" for n in range(26)]
    for name in ["r_dense_features", "ids", *tables, "W_top1", "b_top1", "W_top2", "b_top2", "W_top3"]:
        a = _np.ascontiguousarray(inputs[name])
        arrays[f"in_{name}_dram"] = a
        aps[name] = nc.dram_tensor(f"in_{name}_dram", a.shape, _mybir.dt.from_np(a.dtype), kind="ExternalInput").ap()
    out = nc.dram_tensor("out_dram", (inputs["r_dense_features"].shape[0], 1), F32, kind="ExternalOutput").ap()
    dlrm_tower(nc, aps["r_dense_features"], aps["ids"], [aps[n] for n in tables], aps["W_top1"], aps["b_top1"],
               aps["W_top2"], aps["b_top2"], aps["W_top3"], out)
    r = _run(nc, [arrays], core_ids=[0])
    return r.results[0]["out_dram"]
```

```python
from contextlib import ExitStack

import concourse.bass as bass
from concourse import mybir

F32 = mybir.dt.float32
F32R = mybir.dt.float32r
I32 = mybir.dt.int32
ALU = mybir.AluOpType
ACT = mybir.ActivationFunctionType
AX = mybir.AxisListType

P = 128
SLOTS = 32

ONEHOT = [10, 11, 16, 17, 18, 4]
DOTS_FROM = 20
GROUPS = [[[(0, 4)], [(19, 4)], [(23, 4)], [(4, 4)], [(12, 4)], [(8, 2)]],
          [[(0, 4)], [(19, 4)], [(23, 4)], [(5, 3)], [(12, 4)], [(8, 2)]]]


def features(group):
    return [f + k for f, n in group for k in range(n)]


ORDER = [
    "h h g0 h g1 h g2 h g3-5",
    "u0-1 h u2-3 g0 h g1 h g2 h g3 h g4-5",
    "u0-3 g0 h x0 l0:0 l1:0 g1 l2:0 l3:0 g2 e0 g3 d0-2:2 x1 l0:1 l1:1 g4 d3-5:2 l2:1 g5 l3:1 e1",
    "u0-3 p2 d0-5:3 g0 x2 l0:2 g1 l1:2 g2 l2:2 g3 l3:2 e2 g4 g5",
    "u0-3 p3 x3 l0-3:3 e3",
]


def half_of(m):
    n0 = len(ONEHOT) - 1
    return (0, m) if m < n0 else (1, m - n0)


def plan_steps():
    steps, hots = [], 0
    for t, line in enumerate(ORDER, -1):
        for word in line.split():
            kind, what = word[0], word[1:]
            what, _, tile = what.partition(":")
            first, _, last = what.partition("-")
            for n in range(int(first or 0), int(last or first or 0) + 1):
                if kind == "h":
                    steps.append(("hot", *half_of(hots)))
                    hots += 1
                else:
                    steps.append({"g": ("group", t + 1, n), "u": ("gram", t, n),
                                  "l": ("l1", int(tile or 0), n), "e": ("end", n),
                                  "d": ("dot", int(tile or 0), n), "p": ("pairs", n), "x": ("x", n)}[kind])
    return steps


def dlrm_tower(nc, dense, ids, tables, w1, b1, w2, b2, w3, out):
    B, D = dense.shape
    NF = len(tables) + 1
    N1, N2 = w2.shape
    T = B // P
    HT = T // 2
    HB = HT * P
    NCOL = NF - 1
    NQ = (NCOL + 3) // 4
    GB = 4
    UG = 8
    UB = GB * UG
    NU = P // UB
    GC = GB * NCOL
    BK = 512
    NOHS = (len(ONEHOT) - 1, len(ONEHOT))
    R8 = 8
    RP = tables[ONEHOT[0] - 1].shape[0] // R8
    NG = len(GROUPS[0])
    NPAIR = NF * (NF - 1) // 2
    ACT_ONLY = 1
    ND = 2
    ACT_CHUNKS = (2, 4, 7)
    OHB = 16
    RAW = 2
    gathered = [f for g in GROUPS[0] for f in features(g) if f]
    assert D == P and N1 == BK and sorted(gathered + ONEHOT[:-1]) == list(range(1, NF))
    assert all(tables[f - 1].shape[0] == R8 * RP for f in ONEHOT) and w1.shape[0] == 2 * D + NPAIR

    assert {f for g in GROUPS[1] for f in features(g) if f} == set(gathered) - set(ONEHOT)

    steps = plan_steps()
    banked = [s for s in steps if s[0] in ("hot", "group", "pairs")]

    def bank_of(s):
        return banked.index(s) % 2

    def stored_by_act(s):
        return s[0] != "group" or s[1] >= 1 or s[2] not in (0, 2)

    def stored_count(s):
        return sum(stored_by_act(b) == stored_by_act(s) for b in banked[:banked.index(s) + 1])

    def pair_row(i):
        return D + i * NF - i * (i + 1) // 2

    NB = N1 // P
    KF = 4
    FOLDED_ONES = 3 * P // 4 + NF - 1 - 4 * KF

    def folds():
        for r in range(4):
            at = P // 4 * r
            k, top = KF, 4 * KF + 1
            if r == 0:
                yield k, k + 1, at + top, NF - top, KF - 1, at
                yield k + 1, k + 2, at + top + 4, NF - top - 4, KF - 2, at
            else:
                yield k, k + 2, at + top, NF - top, KF - 2, at
            if 4 * (KF + 2) + r < NCOL:
                yield k + 2, k + 3, at + top + 8, NF - top - 8, KF - 3, at

    def fold_to(i):
        for k0, k1, src, _, to, at in folds():
            if k0 <= i // 4 < k1 and src // 32 == i % 4:
                return to + i // 4 - k0, at + 32 * (i % 4) + i + 1 - src

    assert all(m <= 4 * (to + k - k0) + at // 32 + 1 for k0, k1, _, m, to, at in folds() for k in range(k0, k1))
    PACKS = len(list(folds())) + 1

    NDOT = NF - 1 - DOTS_FROM
    PARTS = []
    for first, n in ((0, NDOT // 2), (NDOT // 2, NDOT - NDOT // 2)):
        PARTS.append((first, n, sum(NDOT - i for i in range(first, first + n)), P // 4 * len(PARTS)))
    ONES_AT = PARTS[1][3] + PARTS[1][2]
    NPD = ONES_AT + 1
    assert DOTS_FROM == 4 * KF + 4 and PARTS[0][2] <= 4 * KF + 1 and NPD - PARTS[1][3] <= 4 * KF + 2
    dot_rows = gathered.index(DOTS_FROM)
    assert gathered[dot_rows:dot_rows + NDOT + 1] == list(range(DOTS_FROM, NF))

    def dot_at(i):
        first, _, _, at = PARTS[i >= PARTS[1][0]]
        return at + sum(NDOT - k for k in range(first, i))

    def dots_done(t, i, a):
        def parts(m):
            return -(-(NDOT - m) // (NDOT // 2))
        return (t - ND) * sum(map(parts, range(NDOT))) + sum(map(parts, range(i))) + a // (NDOT // 2)

    def act_stores(t, q):
        return q >= (0, 2, 2, 2)[t]

    def act_builds(h, c):
        return h == 0 and c in ACT_CHUNKS

    def chunks_built(h, n, c, on_act):
        return sum(act_builds(a, k) == on_act
                   for a in range(h + 1) for m in range(NOHS[0] if a < h else n + 1)
                   for k in range(R8 if (a, m) != (h, n) else c + 1))

    def next_hot(s):
        m = s[1] * NOHS[0] + s[2] + 1
        return half_of(m) if m < sum(NOHS) else None

    def groups_of(t):
        return GROUPS[t // HT]

    def chunk_no(h, n, c):
        return (h * NOHS[0] + n) * R8 + c

    with ExitStack() as ctx:
        def sb(name, shape, dt=F32):
            return ctx.enter_context(nc.sbuf_tensor(name, shape, dt))

        def sem(name):
            return ctx.enter_context(nc.semaphore(name))

        ids_i = sb("ids_i", [P, T, NF - 1], I32)
        ids_f = sb("ids_f", [P, T, NF - 1])
        ids_t = sb("ids_t", [NF - 1, B], F32R)
        x_rows = sb("x_rows", [P, T, D])
        rows = sb("rows", [P, 2, len(gathered), D])
        emb_t = sb("emb_t", [P, T, P, SLOTS])
        z = sb("z", [P, 2, NQ, P])
        w_pair = sb("w_pair", [P, KF + 1, N1])
        w_fold = sb("w_fold", [P, KF, N1])
        prod = sb("prod", [P, NDOT // 2, D])
        dots = sb("dots", [P, 2, NPD])
        w_x = sb("w_x", [P, N1])
        w_2 = sb("w_2", [P, N1 // P, N2])
        w_3 = sb("w_3", [P, N2])
        b_2 = sb("b_2", [1, N2])
        b_2s = sb("b_2s", [1, 2, N2], F32R)
        ones = sb("ones", [1, P])
        ones_r = sb("ones_r", [1, P], F32R)
        zeros = sb("zeros", [P, 1])
        ident = sb("ident", [P, P])
        ident_r = sb("ident_r", [NF - 1, NF - 1], F32R)
        row_i = sb("row_i", [P, R8], I32)
        row_no = sb("row_no", [P, R8])
        neg_row = sb("neg_row", [P, R8])
        tab = sb("tab", [P, RAW, R8, D])
        tab_hi = sb("tab_hi", [P, NOHS[1], R8, D], F32R)
        tab_lo = sb("tab_lo", [P, NOHS[1], R8, D], F32R)
        hot = sb("hot", [P, OHB, HB], F32R)
        away = sb("away", [P, 2, HB])
        h1_t = sb("h1_t", [P, 2, NB, P])
        w_xb = h1_t[:, 1].rearrange("p c b -> p (c b)")
        h2w = sb("h2w", [P, N2])
        y = sb("y", [P, T])

        ps = ctx.enter_context(nc.psum_tensor("ps", [P, 8, BK], F32))
        ROT, GRAM, H = 0, 2, 6
        IDV, IDA = (2, 6), 4

        ids_in = sem("ids_in")
        x_in = sem("x_in")
        tab_in = [sem(f"tab_in{n}") for n in range(NOHS[1])]
        w_pair_in = sem("w_pair_in")
        w_fold_in = sem("w_fold_in")
        folded = [sem(f"folded{t}") for t in range(ND)]
        w_x_in = sem("w_x_in")
        w_2_in = sem("w_2_in")
        small_in = sem("small_in")
        rows_in = [[sem(f"rows_in{t}_{g}") for g in range(NG)] for t in range(T)]
        y_out = sem("y_out")

        zeros_ready = sem("zeros_ready")
        w_pair_zeroed = sem("w_pair_zeroed")
        ident_zeroed = sem("ident_zeroed")
        ident_ready = sem("ident_ready")
        row_i_ready = sem("row_i_ready")
        row_no_ready = sem("row_no_ready")
        pads_ready = sem("pads_ready")
        ids_f_ready = sem("ids_f_ready")
        ids_t_ps = sem("ids_t_ps")
        ids_t_ready = sem("ids_t_ready")
        w_x_ready = sem("w_x_ready")
        b_2_hi_ready = sem("b_2_hi_ready")
        b_2_ready = sem("b_2_ready")
        ids_bc_dve = sem("ids_bc_dve")
        ids_bc_act = sem("ids_bc_act")
        hi_ready = sem("hi_ready")
        lo_ready = sem("lo_ready")
        hot_dve = sem("hot_dve")
        away_ready = sem("away_ready")
        hot_act = sem("hot_act")
        hot_used = sem("hot_used")
        group_ps = sem("group_ps")
        stored_dve = sem("stored_dve")
        stored_act = sem("stored_act")
        gram_ps = sem("gram_ps")
        z_dve = sem("z_dve")
        z_act = sem("z_act")
        prod_ready = sem("prod_ready")
        dots_ready = sem("dots_ready")
        dots_ps = sem("dots_ps")
        l1_ps = sem("l1_ps")
        h1_ready = sem("h1_ready")
        l2_ps = sem("l2_ps")
        y_ready = sem("y_ready")

        def wait_stored(eng, s):
            eng.wait_ge(stored_act if stored_by_act(s) else stored_dve, stored_count(s))

        def wait_z(eng, units):
            eng.wait_ge(z_act, units)
            if units > ACT_ONLY * NU:
                eng.wait_ge(z_dve, units - ACT_ONLY * NU)

        def wait_z_free(eng, t):
            eng.wait_ge(l1_ps, (t - 1) * NB)

        def z_copies(t, u):
            bank = GRAM + 2 * (u % 2)
            for q in range(GB):
                for r in range(4):
                    cols = NCOL if t < ND else DOTS_FROM
                    nq = len(range(r, cols, 4))
                    src = ps[32 * q:32 * q + SLOTS, bank:bank + 2, 0:4 * GC].rearrange(
                        "p k (g c) -> p k g c", g=4)[:, :, :, q * NCOL + r:q * NCOL + cols:4]
                    dst = z[32 * r:32 * r + SLOTS, t % 2, 0:nq, u * UB:(u + 1) * UB].rearrange(
                        "p n (k g b) -> p k g b n", k=2, b=GB)[:, :, :, q, :]
                    yield q, src, dst

        def block_ps(c):
            return ps[:, H + c % 2, c // 2 * P:(c // 2 + 1) * P]

        def group_copies(s):
            _, t, g = s
            m = 0
            for f0, n in groups_of(t)[g]:
                yield (emb_t[:, t, :, f0:f0 + n],
                       ps[:, ROT + bank_of(s), m * P:(m + n) * P].rearrange("p (f b) -> p b f", f=n))
                m += n

        block = ctx.enter_context(nc.Block())

        @block.sync
        def _(sp):
            sp.dma_start(ids_i[:], ids.rearrange("(t p) f -> p t f", p=P)).then_inc(ids_in, 16)

            def load_table(n):
                if n >= RAW:
                    sp.wait_ge(lo_ready, n - RAW + 1)
                f = ONEHOT[n]
                sp.dma_start(tab[0:RP, n % RAW], tables[f - 1].rearrange("(p c) d -> p c d", c=R8)).then_inc(tab_in[n], 16)

            for n in range(NOHS[0]):
                load_table(n)
            sp.dma_start(w_x[:], w1[0:D, :]).then_inc(w_x_in, 16)
            sp.dma_start(w_xb, w1[D + NPAIR:, :]).then_inc(w_x_in, 16)
            sp.dma_start(w_2[:], w2.rearrange("(c p) n -> p c n", p=P)).then_inc(w_2_in, 16)
            sp.dma_start(b_2[:], b2.rearrange("(a n) -> a n", a=1)).then_inc(small_in, 16)
            sp.dma_start(w_3[:], w3.rearrange("n a -> a n").to_broadcast([P, N2])).then_inc(small_in, 16)
            sp.wait_ge(w_pair_zeroed, 1)
            for i in range(DOTS_FROM):
                at = 32 * (i % 4)
                sp.dma_start(w_pair[at + i + 1:at + NF, i // 4, :],
                             w1[pair_row(i):pair_row(i) + NF - 1 - i, :]).then_inc(w_pair_in, 16)
            for first, _, n, at in PARTS:
                w0 = pair_row(DOTS_FROM + first)
                sp.dma_start(w_pair[at:at + n, KF, :], w1[w0:w0 + n, :]).then_inc(w_pair_in, 16)
            sp.dma_start(w_pair[ONES_AT:NPD, KF, :], b1.rearrange("(a n) -> a n", a=1)).then_inc(w_pair_in, 16)
            load_table(NOHS[0])
            sp.wait_ge(w_pair_in, 16 * (DOTS_FROM + 3))
            sp.dma_start(w_fold[:], w_pair[:, 0:KF, :]).then_inc(w_fold_in, 16)
            sp.wait_ge(w_fold_in, 16)
            for i in range(4 * KF, NCOL):
                k, at = fold_to(i)
                sp.dma_start(w_fold[at:at + NF - 1 - i, k, :],
                             w1[pair_row(i):pair_row(i) + NF - 1 - i, :]).then_inc(w_fold_in, 16)
            sp.dma_start(w_fold[FOLDED_ONES:FOLDED_ONES + 1, KF - 1, :], b1.rearrange("(a n) -> a n", a=1)).then_inc(w_fold_in, 16)
            for t in range(ND):
                wait_z(sp, (t + 1) * NU)
                for k0, k1, src, m, to, at in folds():
                    sp.dma_start(z[at:at + m, t % 2, to:to + k1 - k0, :],
                                 z[src:src + m, t % 2, k0:k1, :]).then_inc(folded[t], 16)
                at = 32 * (NCOL % 4)
                sp.dma_start(z[FOLDED_ONES:FOLDED_ONES + 1, t % 2, KF - 1, :],
                             z[at:at + 1, t % 2, NQ - 1, :]).then_inc(folded[t], 16)
            for t in range(T):
                sp.wait_ge(y_ready, t + 1)
                sp.dma_start(out[t * P:(t + 1) * P, :], y[:, t:t + 1]).then_inc(y_out, 16)
            sp.wait_ge(y_out, 16 * T)

        @block.gpsimd
        def _(pool):
            nc.gpsimd.memset(ident[:], 0.0).then_inc(ident_zeroed, 1)
            nc.gpsimd.iota(row_i[:], pattern=[[1, R8]], base=0, channel_multiplier=R8).then_inc(row_i_ready, 1)
            pool.wait_ge(ident_zeroed, 1)
            nc.gpsimd.affine_select(out=ident[:], in_=ident[:], compare_op=ALU.not_equal, fill=1.0, base=0,
                                    pattern=[[-1, P]], channel_multiplier=1).then_inc(ident_ready, 1)
            pool.wait_ge(ids_in, 16)
            for t in range(T):
                if t >= 2:
                    pool.wait_ge(group_ps, (t - 1) * NG)
                for g, group in enumerate(groups_of(t)):
                    for f in features(group):
                        if f:
                            pool.indirect_dma_start(
                                out=rows[:, t % 2, gathered.index(f), :], out_offset=None, in_=tables[f - 1],
                                in_offset=bass.IndirectOffsetOnAxis(ids_i[:, t, f - 1:f], 0),
                            ).then_inc(rows_in[t][g], 16)

        @block.scalar
        def _(act):
            act.dma_start(x_rows[:], dense.rearrange("(t p) d -> p t d", p=P)).then_inc(x_in, 16)
            act.wait_ge(zeros_ready, 1)
            nc.scalar.copy(w_pair[:].rearrange("p k n -> p (k n)"),
                           zeros[:].to_broadcast([P, (KF + 1) * N1])).then_inc(w_pair_zeroed, 1)

            def split_hi(n):
                act.wait_ge(tab_in[n], 16)
                nc.scalar.copy(tab_hi[0:RP, n], tab[0:RP, n % RAW]).then_inc(hi_ready, 1)

            def build_hots(h, n):
                act.wait_ge(ids_bc_act, n + 1)

                def one_hot(c):
                    a = chunks_built(h, n, c, True)
                    act.wait_ge(away_ready, a)
                    k = chunk_no(h, n, c)
                    if k >= OHB:
                        act.wait_ge(hot_used, k - OHB + 1)
                    nc.scalar.activation(hot[0:RP, k % OHB], away[0:RP, a % 2], ACT.Relu, bias=1.0,
                                         scale=-1.0).then_inc(hot_act, 1)

                for m, c in enumerate(ACT_CHUNKS):
                    a = chunks_built(h, n, c, True)
                    if a == 1:
                        act.wait_ge(row_no_ready, 1)
                    if a > 2:
                        act.wait_ge(hot_act, a - 2)
                    nc.scalar.activation(away[0:RP, a % 2], ps[0:RP, IDA + n % 2, 0:HB], ACT.Abs,
                                         bias=neg_row[0:RP, c:c + 1]).then_inc(away_ready, 1)
                    if m:
                        one_hot(ACT_CHUNKS[m - 1])
                one_hot(ACT_CHUNKS[-1])

            def store_hot(s):
                _, h, n = s
                act.wait_ge(hot_used, chunk_no(h, n, R8 - 1) + 1)
                nc.scalar.copy(emb_t[:, h * HT:(h + 1) * HT, :, ONEHOT[n]],
                               ps[:, ROT + bank_of(s), 0:HB].rearrange("p (t b) -> p t b", t=HT)).then_inc(stored_act, 1)

            split_hi(0)
            build_hots(0, 0)
            split_hi(1)
            for s in steps:
                if s[0] == "hot":
                    ahead = next_hot(s)
                    if ahead and ahead[0] == 0:
                        build_hots(*ahead)
                        if ahead[1] + 1 < NOHS[0]:
                            split_hi(ahead[1] + 1)
                    if s == ("hot", 1, 2):
                        split_hi(NOHS[0])
                    store_hot(s)
                if s[0] == "group" and stored_by_act(s):
                    act.wait_ge(group_ps, s[1] * NG + s[2] + 1)
                    copies = list(group_copies(s))
                    for dst, src in copies[:-1]:
                        nc.scalar.copy(dst, src)
                    nc.scalar.copy(*copies[-1]).then_inc(stored_act, 1)
                elif s[0] == "gram":
                    _, t, u = s
                    act.wait_ge(gram_ps, t * NU + u + 1)
                    if u == 0 and t >= 2:
                        wait_z_free(act, t)
                    last = None
                    for q, src, dst in z_copies(t, u):
                        if act_stores(t, q):
                            last = nc.scalar.copy(dst, src)
                    last.then_inc(z_act, 1)
                elif s[0] == "pairs":
                    t = s[1]
                    act.wait_ge(dots_ps, t - ND + 1)
                    wait_z(act, (t + 1) * NU)
                    for _, _, n, at in PARTS:
                        n += at + n == ONES_AT
                        last = nc.scalar.copy(z[at:at + n, t % 2, KF, :], ps[at:at + n, ROT + bank_of(s), 0:P])
                    last.then_inc(stored_act, 1)
                elif s[0] == "l1":
                    _, t, c = s
                    if c == 0 and t >= 2:
                        act.wait_ge(l2_ps, t - 1)
                    act.wait_ge(l1_ps, t * NB + c + 1)
                    nc.scalar.activation(h1_t[:, t % 2, c], block_ps(c), ACT.Relu).then_inc(h1_ready, 1)

        @block.vector
        def _(dve):
            nc.vector.memset(zeros[:], 0.0).then_inc(zeros_ready, 1)
            nc.vector.memset(ones[:], 1.0)
            nc.vector.memset(emb_t[:, 0:HT, :, NF:], 0.0)
            dve.wait_ge(ids_in, 16)
            nc.vector.tensor_copy(ids_f[:], ids_i[:]).then_inc(ids_f_ready, 1)
            dve.wait_ge(ident_ready, 1)
            nc.vector.tensor_copy(ident_r[:], ident[0:NF - 1, 0:NF - 1])
            dve.wait_ge(row_i_ready, 1)
            nc.vector.tensor_scalar(neg_row[:], row_i[:], -1.0, None, ALU.mult)
            nc.vector.tensor_copy(row_no[:], row_i[:]).then_inc(row_no_ready, 1)
            dve.wait_ge(ids_t_ps, 1)
            nc.vector.tensor_copy(ids_t[:], ps[0:NF - 1, IDV[1], :]).then_inc(ids_t_ready, 1)
            dve.wait_ge(row_no_ready, 1)

            def split_lo(n):
                dve.wait_ge(hi_ready, n + 1)
                nc.vector.tensor_tensor(tab_lo[0:RP, n], tab[0:RP, n % RAW], tab_hi[0:RP, n].bitcast(F32),
                                        ALU.subtract).then_inc(lo_ready, 1)

            def build_hots(h, n):
                dve.wait_ge(ids_bc_dve, h * NOHS[0] + n + 1)
                for c in range(R8):
                    if h == 0 and c == 3:
                        split_lo(n)
                    if not act_builds(h, c):
                        k = chunk_no(h, n, c)
                        if k >= OHB:
                            dve.wait_ge(hot_used, k - OHB + 1)
                        nc.vector.tensor_scalar(hot[0:RP, k % OHB], ps[0:RP, IDV[h] + n % 2, 0:HB], row_no[0:RP, c:c + 1],
                                                None, ALU.is_equal).then_inc(hot_dve, 1)

            build_hots(0, 0)
            nc.vector.memset(emb_t[:, HT:, :, NF:], 0.0)
            nc.vector.memset(dots[:, :, PARTS[0][2]:PARTS[1][3]], 0.0)
            nc.vector.memset(dots[:, :, ONES_AT:], 1.0)
            at = 32 * (NCOL % 4)
            nc.vector.memset(z[at:at + 1, :, NQ - 1, :], 1.0).then_inc(pads_ready, 1)
            for s in steps:
                if s[0] == "hot":
                    if s == ("hot", 1, 3):
                        split_lo(NOHS[0])
                    if next_hot(s):
                        build_hots(*next_hot(s))
                elif s[0] == "group" and not stored_by_act(s):
                    dve.wait_ge(group_ps, s[1] * NG + s[2] + 1)
                    copies = list(group_copies(s))
                    for dst, src in copies[:-1]:
                        nc.vector.tensor_copy(dst, src)
                    nc.vector.tensor_copy(*copies[-1]).then_inc(stored_dve, 1)
                elif s[0] == "gram":
                    _, t, u = s
                    if (t, u) == (0, 0):
                        dve.wait_ge(w_x_in, 32)
                        nc.vector.tensor_tensor(w_x[:], w_x[:], w_xb, ALU.add).then_inc(w_x_ready, 1)
                        dve.wait_ge(small_in, 32)
                        nc.vector.tensor_copy(ones_r[:], ones[:])
                        nc.vector.tensor_copy(b_2s[:, 0], b_2[:]).then_inc(b_2_hi_ready, 1)
                        dve.wait_ge(b_2_hi_ready, 1)
                        nc.vector.tensor_tensor(b_2s[:, 1], b_2[:], b_2s[:, 0].bitcast(F32),
                                                ALU.subtract).then_inc(b_2_ready, 1)
                    if t < ACT_ONLY:
                        continue
                    dve.wait_ge(gram_ps, t * NU + u + 1)
                    if u == 0 and t >= 2:
                        wait_z_free(dve, t)
                    mine = [(dst, src) for q, src, dst in z_copies(t, u) if not act_stores(t, q)]
                    for dst, src in mine[:-1]:
                        nc.vector.tensor_copy(dst, src)
                    nc.vector.tensor_copy(*mine[-1]).then_inc(z_dve, 1)
                elif s[0] == "dot":
                    _, t, i = s
                    if i == 0:
                        for g, group in enumerate(groups_of(t)):
                            if max(features(group)) >= DOTS_FROM:
                                dve.wait_ge(rows_in[t][g], 16 * len(features(group)))
                    left = rows[:, t % 2, dot_rows + i:dot_rows + i + 1, :]
                    for a in range(0, NDOT - i, NDOT // 2):
                        n = min(NDOT // 2, NDOT - i - a)
                        if dots_done(t, i, a):
                            dve.wait_ge(dots_ready, dots_done(t, i, a))
                        right = dot_rows + i + 1 + a
                        nc.vector.tensor_tensor(prod[:, 0:n], left.to_broadcast([P, n, D]), rows[:, t % 2, right:right + n, :],
                                                ALU.mult).then_inc(prod_ready, 1)
                        dve.wait_ge(prod_ready, dots_done(t, i, a) + 1)
                        at = dot_at(i) + a
                        nc.vector.tensor_reduce(out=dots[:, t % 2, at:at + n], in_=prod[:, 0:n],
                                                axis=AX.X, op=ALU.add).then_inc(dots_ready, 1)
                elif s[0] == "end":
                    t = s[1]
                    dve.wait_ge(l2_ps, t + 1)
                    if t >= 1:
                        dve.wait_ge(y_ready, t)
                    nc.vector.scalar_tensor_tensor(out=h2w[:], in0=ps[:, H, BK - N2:], scalar=0.0, in1=w_3[:],
                                                   op0=ALU.max, op1=ALU.mult,
                                                   accum_out=y[:, t:t + 1]).then_inc(y_ready, 1)

        @block.tensor
        def _(pe):
            pe.wait_ge(ids_f_ready, 1)
            pe.wait_ge(ident_ready, 1)
            for t in range(T):
                last = nc.tensor.transpose(ps[0:NF - 1, IDV[1], t * P:(t + 1) * P], ids_f[:, t], ident[:])
            last.then_inc(ids_t_ps, 1)

            def broadcast_ids(h, n):
                f = ONEHOT[n] - 1
                picks = ident_r[:, f:f + 1].to_broadcast([NF - 1, P])
                if n >= 2:
                    pe.wait_ge(hot_dve, chunks_built(h, n - 2, R8 - 1, False))
                    if h == 0:
                        pe.wait_ge(hot_act, chunks_built(0, n - 2, R8 - 1, True))
                cols = ids_t[:, h * HB:(h + 1) * HB]
                nc.tensor.matmul(ps[:, IDV[h] + n % 2, 0:HB], picks, cols, start=True, stop=True).then_inc(ids_bc_dve, 1)
                if h == 0:
                    nc.tensor.matmul(ps[:, IDA + n % 2, 0:HB], picks, cols, start=True, stop=True).then_inc(ids_bc_act, 1)

            def wait_bank(s):
                k = banked.index(s)
                if k >= 2:
                    wait_stored(pe, banked[k - 2])

            def x_part(t, c):
                if t * NB + c >= 2:
                    pe.wait_ge(h1_ready, t * NB + c - 1)
                nc.tensor.matmul(block_ps(c), w_x[:, c * P:(c + 1) * P], emb_t[:, t, :, 0], start=True, stop=False)

            pe.wait_ge(ids_t_ready, 1)
            broadcast_ids(0, 0)
            broadcast_ids(0, 1)
            for s in steps:
                if s[0] == "hot":
                    _, h, n = s
                    wait_bank(s)
                    if h == 0 or n == NOHS[0]:
                        pe.wait_ge(hi_ready, n + 1)
                    bank = ps[:, ROT + bank_of(s), 0:HB]
                    for c in range(R8):
                        on_act = act_builds(h, c)
                        pe.wait_ge(hot_act if on_act else hot_dve, chunks_built(h, n, c, on_act))
                        one_hot = hot[0:RP, chunk_no(h, n, c) % OHB]
                        nc.tensor.matmul(bank, tab_hi[0:RP, n, c], one_hot, start=c == 0, stop=False)
                        if (h == 0 or n == NOHS[0]) and c == 0:
                            pe.wait_ge(lo_ready, n + 1)
                        nc.tensor.matmul(bank, tab_lo[0:RP, n, c], one_hot,
                                         start=False, stop=c == R8 - 1).then_inc(hot_used, 1)
                    m = h * NOHS[0] + n + 2
                    if m < sum(NOHS):
                        broadcast_ids(*half_of(m))
                elif s[0] == "group":
                    _, t, g = s
                    feats = features(groups_of(t)[g])
                    if 0 in feats:
                        pe.wait_ge(x_in, 16)
                    pe.wait_ge(rows_in[t][g], 16 * (len(feats) - (0 in feats)))
                    wait_bank(s)
                    for m, f in enumerate(feats):
                        src = rows[:, t % 2, gathered.index(f), :] if f else x_rows[:, t]
                        last = nc.tensor.transpose(ps[:, ROT + bank_of(s), m * P:(m + 1) * P], src, ident[:])
                    last.then_inc(group_ps, 1)
                elif s[0] == "gram":
                    _, t, u = s
                    if u == 0:
                        if t == 0:
                            pe.wait_ge(pads_ready, 1)
                        for b in [("group", t, g) for g in range(NG)] + [("hot", t // HT, NOHS[t // HT] - 1)]:
                            wait_stored(pe, b)
                        if t == 0:
                            pe.wait_ge(hot_dve, chunks_built(0, NOHS[0] - 1, R8 - 1, False))
                            pe.wait_ge(hot_act, chunks_built(0, NOHS[0] - 1, R8 - 1, True))
                    k = t * NU + u
                    if k >= 2:
                        wait_z(pe, k - 1)
                    for g in range(UG):
                        b0 = u * UB + g * GB
                        last = nc.tensor.matmul(ps[:, GRAM + 2 * (u % 2) + g // 4, g % 4 * GC:(g % 4 + 1) * GC],
                                                emb_t[:, t, b0:b0 + GB, :].rearrange("p b f -> p (b f)"),
                                                emb_t[:, t, b0:b0 + GB, 0:NCOL], start=True, stop=True)
                    last.then_inc(gram_ps, 1)
                elif s[0] == "pairs":
                    t = s[1]
                    pe.wait_ge(dots_ready, dots_done(t + 1, 0, 0))
                    wait_bank(s)
                    nc.tensor.transpose(ps[0:NPD, ROT + bank_of(s), 0:P], dots[:, t % 2], ident[:]).then_inc(dots_ps, 1)
                elif s[0] == "x":
                    t = s[1]
                    if t == 0:
                        pe.wait_ge(hot_dve, chunks_built(1, NOHS[1] - 1, R8 - 1, False))
                        pe.wait_ge(w_x_ready, 1)
                        pe.wait_ge(w_fold_in, 16 * (NCOL - 4 * KF + 2))
                    if t == ND:
                        pe.wait_ge(w_pair_in, 16 * (DOTS_FROM + 3))
                    x_part(t, 1)
                    if t >= 1:
                        pe.wait_ge(y_ready, t)
                    x_part(t, 0)
                elif s[0] == "l1":
                    _, t, c = s
                    cols = slice(c * P, (c + 1) * P)
                    if c >= 2:
                        x_part(t, c)
                    elif c == 0 and t < ND:
                        pe.wait_ge(folded[t], 16 * PACKS)
                    elif c == 0:
                        wait_z(pe, (t + 1) * NU)
                    weights, nk = (w_fold, KF) if t < ND else (w_pair, KF + 1)
                    for k in range(nk):
                        if (c, k) == (0, KF):
                            wait_stored(pe, ("pairs", t))
                        last = nc.tensor.matmul(block_ps(c), weights[:, k, cols], z[:, t % 2, k, :],
                                                start=False, stop=k == nk - 1)
                    last.then_inc(l1_ps, 1)
                elif s[0] == "end":
                    t = s[1]
                    if t == 0:
                        pe.wait_ge(w_2_in, 16)
                        pe.wait_ge(b_2_ready, 1)
                    sums = ps[:, H, BK - N2:]
                    pe.wait_ge(h1_ready, t * NB + NB - 1)
                    nc.tensor.matmul(sums, ones_r[:], b_2s[:, 0], start=True, stop=False)
                    nc.tensor.matmul(sums, ones_r[:], b_2s[:, 1], start=False, stop=False)
                    for c in range(NB):
                        pe.wait_ge(h1_ready, t * NB + c + 1)
                        last = nc.tensor.matmul(sums, h1_t[:, t % 2, c], w_2[:, c], start=False, stop=c == NB - 1)
                    last.then_inc(l2_ps, 1)


def kernel(**inputs):
    import numpy as _np
    import concourse.bacc as _bacc
    from concourse import mybir as _mybir
    from concourse.bass_utils import run_bass_kernel_spmd as _run

    nc = _bacc.Bacc("TRN2", target_bir_lowering=False, num_devices=1)
    arrays, aps = {}, {}
    tables = [f"tbl_{n}" for n in range(26)]
    for name in ["r_dense_features", "ids", *tables, "W_top1", "b_top1", "W_top2", "b_top2", "W_top3"]:
        a = _np.ascontiguousarray(inputs[name])
        arrays[f"in_{name}_dram"] = a
        aps[name] = nc.dram_tensor(f"in_{name}_dram", a.shape, _mybir.dt.from_np(a.dtype), kind="ExternalInput").ap()
    out = nc.dram_tensor("out_dram", (inputs["r_dense_features"].shape[0], 1), F32, kind="ExternalOutput").ap()
    dlrm_tower(nc, aps["r_dense_features"], aps["ids"], [aps[n] for n in tables], aps["W_top1"], aps["b_top1"],
               aps["W_top2"], aps["b_top2"], aps["W_top3"], out)
    r = _run(nc, [arrays], core_ids=[0])
    return r.results[0]["out_dram"]
```
